# Optimizing a Trainium2 kernel written in Bass

```python
import numpy as np
import jax
import jax.numpy as jnp

def _softmax(x, axis=-1):
    return jax.nn.softmax(x, axis=axis)

def _gelu(x):
    return jax.nn.gelu(x, approximate=True)

def _silu(x):
    return jax.nn.silu(x)

def _sigmoid(x):
    return jax.nn.sigmoid(x)

def _layernorm(x, axis=-1, eps=1e-05):
    m = jnp.mean(x, axis=axis, keepdims=True)
    v = jnp.var(x, axis=axis, keepdims=True)
    return (x - m) / jnp.sqrt(v + eps)

def _scatter_add(tgt, idx, src, axis=0):
    return tgt.at[idx].add(src)

def _segment_sum(src, seg, n):
    return jax.ops.segment_sum(src, seg, n)
kernel_name = 'mk_xattn_ffn_d2_seqx_r4_0ce821'

def setup_inputs(seed: int=0):
    np.random.seed(seed)
    _w = jnp.asarray

    def _rec_inputs():
        import jax
        import jax.numpy as jnp
        _rk = jax.random.key(seed)
        x = -0.0005207 + 1.001 * jax.random.normal(jax.random.fold_in(_rk, 1), (2, 512, 512), jnp.float32)
        _lenS = 512 - jax.random.randint(jax.random.fold_in(_rk, 7), (2,), 0, max(1, 512 // 4) + 1, jnp.int32)
        _lenS2 = 1024 - jax.random.randint(jax.random.fold_in(_rk, 8), (2,), 0, max(1, 1024 // 4) + 1, jnp.int32)
        _ctx_2048P = jax.random.normal(jax.random.fold_in(_rk, 12), (2, 16, 512), jnp.float32)
        _ctx_2048c = jax.random.dirichlet(jax.random.fold_in(_rk, 512), 0.3 * jnp.ones((16,), jnp.float32), (2, 1024))
        _ctx_2048t = jnp.einsum('bsk,bkd->bsd', _ctx_2048c, _ctx_2048P)
        _ctx_2048t = _ctx_2048t * jax.lax.rsqrt(jnp.mean(jnp.square(_ctx_2048t)) + 1e-12) * 0.953939
        ctx_2048 = -5.72187e-05 + 0.999849 * (_ctx_2048t + 0.3 * jax.random.normal(jax.random.fold_in(_rk, 612), (2, 1024, 512), jnp.float32))
        _validS = jnp.arange(512)[None, :] < _lenS[:, None]
        _validS2 = jnp.arange(1024)[None, :] < _lenS2[:, None]
        _causal = jnp.tril(jnp.ones((512, 512), dtype=bool))
        mask_BxSx4224_bf0 = jnp.logical_not(jnp.ones((2, 512, 1056), dtype=bool))
        mask_BxS2_bk0 = jnp.logical_not(jnp.broadcast_to(_validS2[:, :], (2, 1024)))
        return (x, ctx_2048, mask_BxSx4224_bf0, mask_BxS2_bk0)
    x, ctx_2048, mask_BxSx4224_bf0, mask_BxS2_bk0 = _rec_inputs()

    def _L0_xattn_setup():
        import jax, jax.numpy as jnp
        import numpy as np
        import math
        DIM = 512
        B, Q_LEN, KV_LEN = (8, 128, 1024)
        key = jax.random.key(seed)
        ks = jax.random.split(key, 8)
        x = jax.random.normal(ks[0], (B, Q_LEN, DIM), dtype=jnp.float32)
        mask = jnp.zeros((B, Q_LEN, KV_LEN + Q_LEN), dtype=bool)
        k_cache = jax.random.normal(ks[1], (B, KV_LEN, DIM), dtype=jnp.float32)
        v_cache = jax.random.normal(ks[2], (B, KV_LEN, DIM), dtype=jnp.float32)
        scale = 1.0 / math.sqrt(DIM)
        wq = jax.random.normal(ks[3], (DIM, DIM), dtype=jnp.float32) * scale
        wk = jax.random.normal(ks[4], (DIM, DIM), dtype=jnp.float32) * scale
        wv = jax.random.normal(ks[5], (DIM, DIM), dtype=jnp.float32) * scale
        wo = jax.random.normal(ks[6], (DIM, DIM), dtype=jnp.float32) * scale
        return {'x': x, 'mask': mask, 'k_cache': k_cache, 'v_cache': v_cache, 'wq': wq, 'wk': wk, 'wv': wv, 'wo': wo}
    _L0_xattn_all = _L0_xattn_setup()
    _L0_xattn_in = {k: v for k, v in _L0_xattn_all.items() if k in ('wq', 'wk', 'wv', 'wo')}
    del _L0_xattn_all

    def _L0_ffn_setup():
        import jax, jax.numpy as jnp
        import numpy as np
        B, S, D = (4, 512, 512)
        E, K, M = (8, 2, 256)
        key = jax.random.key(seed)
        k0, k1, k2, k3, k4 = jax.random.split(key, 5)
        d_scale = D ** (-0.5)
        m_scale = M ** (-0.5)
        return {'x': jax.random.normal(k0, (B, S, D), jnp.float32), 'w_gate': jax.random.normal(k1, (D, E), jnp.float32) * d_scale, 'wi_0': jax.random.normal(k2, (E, D, M), jnp.float32) * d_scale, 'wi_1': jax.random.normal(k3, (E, D, M), jnp.float32) * d_scale, 'wo': jax.random.normal(k4, (E, M, D), jnp.float32) * m_scale}
    _L0_ffn_all = _L0_ffn_setup()
    _L0_ffn_in = {k: v for k, v in _L0_ffn_all.items() if k in ('w_gate', 'wi_0', 'wi_1', 'wo')}
    del _L0_ffn_all

    def _L1_xattn_setup():
        import jax, jax.numpy as jnp
        import numpy as np
        key = jax.random.key(seed)
        k1, k2, k3 = jax.random.split(key, 3)
        B, S, D, M = (8, 512, 512, 128)
        hidden_states = jax.random.normal(k1, (B, S, D), dtype=jnp.float32)
        memory_tokens = jax.random.normal(k2, (B, M, D), dtype=jnp.float32)
        memory_mask = jax.random.randint(k3, (B, M), 0, 2).astype(jnp.bool_)
        return {'hidden_states': hidden_states, 'memory_tokens': memory_tokens, 'memory_mask': memory_mask}
    _L1_xattn_all = _L1_xattn_setup()
    _L1_xattn_in = {k: v for k, v in _L1_xattn_all.items() if k in ()}
    del _L1_xattn_all

    def _L1_ffn_setup():
        import jax, jax.numpy as jnp
        import numpy as np
        TOP_K = 8
        NORM_TOPK_PROB = True
        key = jax.random.key(seed)
        k1, k2, k3, k4, k5 = jax.random.split(key, 5)
        B, S, H, E, I = (2, 512, 512, 32, 192)
        scale = 0.02
        return {'x': jax.random.normal(k1, (B, S, H), dtype=jnp.float32), 'gate_w': jax.random.normal(k2, (E, H), dtype=jnp.float32) * scale, 'w_gate': jax.random.normal(k3, (E, H, I), dtype=jnp.float32) * scale, 'w_up': jax.random.normal(k4, (E, H, I), dtype=jnp.float32) * scale, 'w_down': jax.random.normal(k5, (E, I, H), dtype=jnp.float32) * scale}
    _L1_ffn_all = _L1_ffn_setup()
    _L1_ffn_in = {k: v for k, v in _L1_ffn_all.items() if k in ('gate_w', 'w_gate', 'w_up', 'w_down')}
    del _L1_ffn_all
    return {'x': x, 'ctx_2048': ctx_2048, 'mask_BxSx4224_bf0': mask_BxSx4224_bf0, 'mask_BxS2_bk0': mask_BxS2_bk0, 'L0_xattn_wq': _L0_xattn_in['wq'], 'L0_xattn_wk': _L0_xattn_in['wk'], 'L0_xattn_wv': _L0_xattn_in['wv'], 'L0_xattn_wo': _L0_xattn_in['wo'], 'L0_ffn_w_gate': _L0_ffn_in['w_gate'], 'L0_ffn_wi_0': _L0_ffn_in['wi_0'], 'L0_ffn_wi_1': _L0_ffn_in['wi_1'], 'L0_ffn_wo': _L0_ffn_in['wo'], 'L1_ffn_gate_w': _L1_ffn_in['gate_w'], 'L1_ffn_w_gate': _L1_ffn_in['w_gate'], 'L1_ffn_w_up': _L1_ffn_in['w_up'], 'L1_ffn_w_down': _L1_ffn_in['w_down']}

def reference(x, ctx_2048, mask_BxSx4224_bf0, mask_BxS2_bk0, L0_xattn_wq, L0_xattn_wk, L0_xattn_wv, L0_xattn_wo, L0_ffn_w_gate, L0_ffn_wi_0, L0_ffn_wi_1, L0_ffn_wo, L1_ffn_gate_w, L1_ffn_w_gate, L1_ffn_w_up, L1_ffn_w_down):
    import jax
    import jax.numpy as jnp

    def _L0_xattn_ref(x, mask, k_cache, v_cache, wq, wk, wv, wo):
        import jax, jax.numpy as jnp
        import numpy as np
        import math
        DIM = 512
        B, Q_LEN, KV_LEN = (8, 128, 1024)
        q = jnp.einsum('bsd,ed->bse', x, wq)
        k_new = jnp.einsum('bsd,ed->bse', x, wk)
        v_new = jnp.einsum('bsd,ed->bse', x, wv)
        k = jnp.concatenate([k_cache, k_new], axis=1)
        v = jnp.concatenate([v_cache, v_new], axis=1)
        scale = 1.0 / math.sqrt(q.shape[-1])
        scores = jnp.einsum('bqd,bkd->bqk', q, k) * scale
        attn = jax.nn.softmax(scores, axis=-1)
        out = jnp.einsum('bqk,bkd->bqd', attn, v)
        return jnp.einsum('bqd,ed->bqe', out, wo)

    def _L0_ffn_ref(x, w_gate, wi_0, wi_1, wo):
        import jax, jax.numpy as jnp
        import numpy as np
        B, S, D = (4, 512, 512)
        E, K, M = (8, 2, 256)
        b, s, d = x.shape
        e = w_gate.shape[1]
        xf = x.reshape(-1, d)
        logits = jnp.dot(xf, w_gate)
        top_logits, top_idx = jax.lax.top_k(logits, K)
        weights = jax.nn.softmax(top_logits, axis=-1)
        flat_idx = top_idx.reshape(-1)
        sort_order = jnp.argsort(flat_idx)
        token_ids = sort_order // K
        sorted_x = jnp.take(xf, token_ids, axis=0)
        group_sizes = jnp.bincount(flat_idx, length=E).astype(jnp.int32)
        h0 = jax.lax.ragged_dot(sorted_x, wi_0, group_sizes)
        h1 = jax.lax.ragged_dot(sorted_x, wi_1, group_sizes)
        inter = jax.nn.silu(h0) * h1
        out_sorted = jax.lax.ragged_dot(inter, wo, group_sizes)
        unsort = jnp.argsort(sort_order)
        out = jnp.take(out_sorted, unsort, axis=0).reshape(-1, K, d)
        out = jnp.einsum('tkd,tk->td', out, weights)
        return out.reshape(b, s, d)

    def _L1_xattn_ref(hidden_states, memory_tokens, memory_mask):
        import jax, jax.numpy as jnp
        import numpy as np
        B, S, D = hidden_states.shape
        scale = 1.0 / jnp.sqrt(jnp.asarray(D, hidden_states.dtype))
        scores = jnp.einsum('bsd,bmd->bsm', hidden_states, memory_tokens) * scale
        neg_inf = jnp.asarray(-1e+30, scores.dtype)
        scores = jnp.where(memory_mask[:, None, :], scores, neg_inf)
        attn = jax.nn.softmax(scores, axis=-1)
        readout = jnp.einsum('bsm,bmd->bsd', attn, memory_tokens)
        valid_b = jnp.any(memory_mask, axis=-1)
        out = jnp.where(valid_b[:, None, None], readout, jnp.zeros_like(readout))
        return out

    def _L1_ffn_ref(x, gate_w, w_gate, w_up, w_down):
        import jax, jax.numpy as jnp
        import numpy as np
        TOP_K = 8
        NORM_TOPK_PROB = True
        B, S, H = x.shape
        E = gate_w.shape[0]
        xt = x.reshape(-1, H)
        T = xt.shape[0]
        router_logits = xt @ gate_w.T
        routing_weights = jax.nn.softmax(router_logits.astype(jnp.float32), axis=-1)
        top_w, top_idx = jax.lax.top_k(routing_weights, TOP_K)
        rows = jnp.arange(T)[:, None]
        full_w = jnp.zeros_like(routing_weights).at[rows, top_idx].set(top_w)
        if NORM_TOPK_PROB:
            denom = jnp.clip(full_w.sum(axis=-1, keepdims=True), 1e-09, None)
            full_w = full_w / denom
        full_w = full_w.astype(x.dtype)
        g = jax.nn.silu(jnp.einsum('th,ehi->eti', xt, w_gate))
        u = jnp.einsum('th,ehi->eti', xt, w_up)
        y = jnp.einsum('eti,eih->eth', g * u, w_down)
        out = jnp.einsum('eth,te->th', y, full_w)
        return out.reshape(B, S, H)
    x = x + _L0_xattn_ref(_layernorm(x, axis=-1), mask_BxSx4224_bf0, ctx_2048, ctx_2048, L0_xattn_wq, L0_xattn_wk, L0_xattn_wv, L0_xattn_wo)
    x = x + _L0_ffn_ref(_layernorm(x, axis=-1), L0_ffn_w_gate, L0_ffn_wi_0, L0_ffn_wi_1, L0_ffn_wo)
    x = x + _L1_xattn_ref(_layernorm(x, axis=-1), ctx_2048, mask_BxS2_bk0)
    x = x + _L1_ffn_ref(_layernorm(x, axis=-1), L1_ffn_gate_w, L1_ffn_w_gate, L1_ffn_w_up, L1_ffn_w_down)
    return x

_drawn_inputs = setup_inputs


def setup_inputs(seed=0):
    import zlib

    import numpy as np

    out = dict(_drawn_inputs(seed))
    spreads = {}
    factors = {'L1_ffn_gate_w': 7.31, 'L1_ffn_w_gate': 6.303, 'L1_ffn_w_up': 6.166, 'L1_ffn_w_down': 6.16}
    for name, (base, spread) in spreads.items():
        noise = np.random.default_rng([zlib.crc32(name.encode()), seed]).standard_normal(out[name].shape)
        drawn = base * np.exp(spread * noise) if base else spread * noise
        out[name] = jnp.asarray(drawn.astype(out[name].dtype))
    for name, factor in factors.items():
        out[name] = (out[name] * factor).astype(out[name].dtype)
    return out
```

```python
from contextlib import ExitStack

import numpy as np
import concourse.bass as bass
from concourse import mybir

ALU = mybir.AluOpType
ACT = mybir.ActivationFunctionType
F32 = mybir.dt.float32
F16 = mybir.dt.float16
U32 = mybir.dt.uint32
U8 = mybir.dt.uint8
AX_X = mybir.AxisListType.X

P = 128
EPS = 1e-5
NEG = 1e30


def program(nc, x_in, ctx_in, mask_in, wq, wk, wv, wo, g0_in, wi0, wi1, wo0, g1_in, wg1, wu1, wd1, out):
    B, S, D = x_in.shape
    C = ctx_in.shape[1]
    NT = B * S // P
    ND = D // P
    NCT = B * C // P
    TPB = S // P
    CPB = C // P
    E0, _, I0 = wi0.shape
    E1, _, I1 = wg1.shape
    SCALE = float(D) ** -0.5

    ctx = ExitStack()
    with ctx:
        def sem(name):
            return ctx.enter_context(nc.semaphore(name))

        def sb(name, shape, dt):
            return ctx.enter_context(nc.sbuf_tensor(name, shape, dt))

        x_sb = sb("x_sb", [P, NT, D], F32)
        xT = sb("xT", [P, 2, ND, NT * P], F16)
        ctxT = sb("ctxT", [P, 2, ND, NCT * P], F16)
        ctxN = sb("ctxN", [P, 2, NCT, D], F16)
        xn = sb("xn", [P, 2, D], F32)
        id32 = sb("id32", [P, P], F32)
        id16 = sb("id16", [P, P], F16)
        small = sb("small", [P, 64], F32)
        g1T = sb("g1T", [P, 2, ND, E1], F16)
        g0 = sb("g0", [P, 2, ND, E0], F16)

        big = sb("big", [P, 40960], F16)
        mid = sb("mid", [P, 12288], F16)

        def carve(arena, at, elems, dt, pattern=None, **sizes):
            n = elems * (2 if dt in (F32, U32) else 1)
            v = arena[:, at:at + n]
            if dt is not F16:
                v = v.bitcast(dt)
            return v.rearrange(pattern, **sizes) if pattern else v

        W4 = ND * D
        wT = {n: carve(big, i * 2 * W4, 2 * W4, F16, "p (h d e) -> p h d e", h=2, d=ND)
              for i, n in enumerate("qkvo")}
        qT = carve(big, 8 * W4, 2 * ND * NT * P, F16, "p (h d t) -> p h d t", h=2, d=ND)
        kT = carve(big, 12 * W4, 2 * ND * NT * P, F16, "p (h d t) -> p h d t", h=2, d=ND)
        vN = carve(big, 16 * W4, 2 * NT * D, F16, "p (h t d) -> p h t d", h=2, t=NT)
        wraw = [carve(mid, s * 2 * W4, W4, F32, "p (c d) -> p c d", c=ND) for s in range(2)]
        craw = [carve(mid, 4 * W4 + s * 2 * D, D, F32) for s in range(4)]
        KV = 1536
        pf = carve(mid, 0, KV, F32)
        ph = carve(mid, 3072, 2 * KV, F16, "p (h k) -> p h k", h=2)
        pT = carve(mid, 6144, 2 * KV, F16, "p (h k q) -> p h k q", h=2, q=P)
        of = carve(mid, 9216, D, F32)
        oh = carve(mid, 10240, 2 * D, F16, "p (h d) -> p h d", h=2)
        oT = carve(mid, 11264, 2 * D, F16, "p (h d q) -> p h d q", h=2, q=P)
        mraw = carve(big, 36864, 2048 // 2, F16).bitcast(U8).rearrange("p (b c) -> p b c", b=B)
        mbias = carve(big, 36864 - 4096, B * C, F32, "p (b c) -> p b c", b=B)
        mval = small[:, 40:42]

        pst = ctx.enter_context(nc.psum_tensor("pst", [P, 4096], F32))

        def bank(b, n=1):
            return pst[:, 512 * b:512 * (b + n)]

        def bank16(b):
            return bank(b).bitcast(F16)

        rmax, nmax, rsum, rinv = small[:, 10:11], small[:, 12:14], small[:, 14:16], small[:, 16:18]
        stats = sb("stats", [P, NT, 6], F32)
        mv = sb("mv", [P, NT, 2], F32)
        std = sb("std", [P, NT], F32)
        rstd = sb("rstd", [P, NT], F32)

        x_in_s = [sem(f"x_loaded_{i}") for i in range(NT)]
        w_in_s = [sem(f"attn_weight_loaded_{i}") for i in range(2)]
        c_in_s = [sem(f"context_loaded_{i}") for i in range(4)]
        g_in_s = sem("routers_loaded")
        m_in_s = sem("mask_loaded")
        ident_s = sem("identity_ready")
        ident0_s = sem("identity_cleared")
        dve_s = sem("vector_step")
        act_s = sem("scalar_step")
        prep_full = sem("prep_bank_full")
        prep_hi = sem("prep_high_part_out")
        prep_lo = sem("prep_low_part_out")
        ctx_hi = sem("context_rows_high")
        ctx_lo = sem("context_rows_low")
        g0_s = sem("router0_split")
        xn_s = sem("x_normalised")
        var_s = sem("variances_ready")
        std_s = sem("deviations_ready")
        g0r = sb("g0r", [P, ND, E0], F32)
        g1r = carve(big, 16 * W4, D, F32)[0:E1, :]

        prep = [("x", i) for i in range(NT)]
        prep += [("w", n, d) for n in "qk" for d in range(ND)]
        prep += [("proj", "q", c, b) for c in range(ND) for b in range(B)]
        prep += [("w", "v", d) for d in range(ND)]
        prep += [("proj", "k", c, b) for c in range(ND) for b in range(B)]
        prep += [("w", "o", d) for d in range(ND)] + [("g",)]
        prep += [("projv", t) for t in range(NT)]
        prep += [("ctx", k) for k in range(NCT)]
        at = {j: n for n, j in enumerate(prep)}
        NPREP = len(prep)

        def prep_dst(j, h):
            if j[0] == "x":
                return xT[:, h, :, j[1] * P:(j[1] + 1) * P]
            if j[0] == "w":
                return wT[j[1]][:, h, j[2], :]
            if j[0] == "proj":
                return (qT if j[1] == "q" else kT)[:, h, j[2], j[3] * S:(j[3] + 1) * S]
            if j[0] == "projv":
                return vN[:, h, j[1], :]
            if j[0] == "g":
                return g1T[:, h, :, :]
            return ctxT[:, h, :, j[1] * P:(j[1] + 1) * P]

        def prep_src(n):
            j = prep[n]
            v = bank(n % 8)
            if j[0] in ("x", "ctx"):
                return v.rearrange("p (c t) -> p c t", c=ND)
            if j[0] == "g":
                return v[:, 0:ND * E1].rearrange("p (c t) -> p c t", c=ND)
            return v

        PASSES = [(0, 0), (0, 1), (1, 0)]

        def three(pe, dst, parts, stationary, moving):
            k, last = 0, None
            for c in parts:
                for a, b in PASSES:
                    last = nc.tensor.matmul(dst, stationary(a, c), moving(b, c), start=(k == 0),
                                            stop=(k == 3 * len(parts) - 1))
                    k += 1
            return last

        def pe_prep(pe):
            pe.wait_ge(ident_s, 2)
            for n, j in enumerate(prep):
                if n >= 8:
                    pe.wait_ge(prep_lo, n - 7)
                dst = bank(n % 8)
                if j[0] == "x":
                    pe.wait_ge(xn_s, j[1] + 1)
                    for c in range(ND):
                        last = nc.tensor.transpose(dst[:, c * P:(c + 1) * P], xn[:, j[1] % 2, c * P:(c + 1) * P], id32[:])
                elif j[0] == "w":
                    slot, use = {"q": (0, 1), "k": (1, 1), "v": (0, 2), "o": (1, 2)}[j[1]]
                    pe.wait_ge(w_in_s[slot], 16 * use)
                    for c in range(ND):
                        last = nc.tensor.transpose(dst[:, c * P:(c + 1) * P], wraw[slot][:, c, j[2] * P:(j[2] + 1) * P], id32[:])
                elif j[0] == "g":
                    pe.wait_ge(g_in_s, 32)
                    for c in range(ND):
                        last = nc.tensor.transpose(dst[:, c * E1:(c + 1) * E1], g1r[:, c * P:(c + 1) * P], id32[0:E1, 0:E1])
                elif j[0] == "ctx":
                    pe.wait_ge(c_in_s[j[1] % 4], 16 * (j[1] // 4 + 1))
                    for c in range(ND):
                        last = nc.tensor.transpose(dst[:, c * P:(c + 1) * P], craw[j[1] % 4][:, c * P:(c + 1) * P], id32[:])
                elif j[0] == "proj":
                    pe.wait_ge(prep_lo, at[("w", j[1], ND - 1)] + 1)
                    w, c, b = wT[j[1]], j[2], j[3]
                    last = three(pe, dst, range(ND), lambda h, d: w[:, h, d, c * P:(c + 1) * P],
                                 lambda h, d: xT[:, h, d, b * S:(b + 1) * S])
                else:
                    pe.wait_ge(prep_lo, at[("w", "v", ND - 1)] + 1)
                    t = j[1]
                    last = three(pe, dst, range(ND), lambda h, d: xT[:, h, d, t * P:(t + 1) * P],
                                 lambda h, d: wT["v"][:, h, d, :])
                last.then_inc(prep_full, 1)

        def act_prep(act):
            root(act, 0)
            for n, j in enumerate(prep):
                act.wait_ge(prep_full, n + 1)
                nc.scalar.activation(prep_dst(j, 0), prep_src(n), ACT.Copy).then_inc(prep_hi, 1)

        chain = [0]

        def link(dve, ins):
            chain[0] += 1
            ins.then_inc(dve_s, 1)
            dve.wait_ge(dve_s, chain[0])

        def statistics(dve, layer, arrived):
            for i in range(NT):
                arrived(i)
                last = nc.vector.bn_stats(stats[:, i, :], x_sb[:, i, :])
            link(dve, last)
            for i in range(NT):
                last = nc.vector.bn_aggr(mv[:, i, :], stats[:, i, :])
            link(dve, last)
            nc.vector.tensor_scalar(rstd[:], mv[:, :, 1], EPS, None, ALU.add).then_inc(var_s, 1)
            dve.wait_ge(std_s, layer + 1)
            link(dve, nc.vector.reciprocal(rstd[:], std[:]))

        def root(act, layer):
            act.wait_ge(var_s, layer + 1)
            nc.scalar.activation(std[:], rstd[:], ACT.Sqrt).then_inc(std_s, 1)

        def normalise(dve, i, ring_free):
            ring_free()
            nc.vector.tensor_scalar(xn[:, i % 2, :], x_sb[:, i, :], mv[:, i, 0:1], rstd[:, i:i + 1], ALU.subtract,
                                    ALU.mult).then_inc(xn_s, 1)

        def dve_prep(dve):
            def norm(i):
                def ring_free():
                    if i >= 2:
                        dve.wait_ge(prep_full, i - 1)
                normalise(dve, i, ring_free)
            statistics(dve, 0, lambda i: dve.wait_ge(x_in_s[i], 16))
            norm(0)
            norm(1)
            dve.wait_ge(g_in_s, 32)
            link(dve, nc.vector.tensor_copy(g0[:, 0, :, :], g0r[:]))
            nc.vector.tensor_tensor(g0[:, 1, :, :], g0r[:], g0[:, 0, :, :], ALU.subtract).then_inc(g0_s, 1)
            for n, j in enumerate(prep):
                dve.wait_ge(prep_hi, n + 1)
                nc.vector.tensor_tensor(prep_dst(j, 1), prep_src(n), prep_dst(j, 0), ALU.subtract).then_inc(prep_lo, 1)
                if n + 2 < NT:
                    norm(n + 2)

        def pool_prep(pool):
            nc.gpsimd.memset(id32[:], 0.0).then_inc(ident0_s, 1)
            nc.gpsimd.memset(id16[:], 0.0).then_inc(ident0_s, 1)
            pool.wait_ge(ident0_s, 2)
            for m in (id32, id16):
                nc.gpsimd.affine_select(out=m[:], in_=m[:], compare_op=ALU.not_equal, fill=1.0, base=0,
                                        pattern=[[-1, P]], channel_multiplier=1).then_inc(ident_s, 1)
            for k in range(NCT):
                pool.wait_ge(c_in_s[k % 4], 16 * (k // 4 + 1))
                nc.gpsimd.tensor_copy(ctxN[:, 0, k, :], craw[k % 4]).then_inc(ctx_hi, 1)
                pool.wait_ge(ctx_hi, k + 1)
                nc.gpsimd.tensor_tensor(ctxN[:, 1, k, :], craw[k % 4], ctxN[:, 0, k, :], ALU.subtract).then_inc(ctx_lo, 1)

        def sp_prep(sp):
            xt = x_in.rearrange("b (t p) d -> p (b t) d", p=P)
            ct = ctx_in.rearrange("b (t p) d -> p (b t) d", p=P)

            def wload(slot, w):
                sp.dma_start(wraw[slot], w.rearrange("(c p) d -> p c d", p=P)).then_inc(w_in_s[slot], 16)
            for i in range(NT):
                sp.dma_start(x_sb[:, i, :], xt[:, i, :]).then_inc(x_in_s[i], 16)
            sp.dma_start(g0r[:], g0_in.rearrange("(c p) e -> p c e", p=P)).then_inc(g_in_s, 16)
            sp.dma_start(g1r[:], g1_in).then_inc(g_in_s, 16)
            wload(0, wq)
            wload(1, wk)
            for k in range(NCT):
                if k == 4:
                    sp.wait_ge(prep_full, at[("w", "q", ND - 1)] + 1)
                    wload(0, wv)
                    sp.wait_ge(prep_full, at[("w", "k", ND - 1)] + 1)
                    wload(1, wo)
                if k >= 4:
                    sp.wait_ge(prep_full, at[("ctx", k - 4)] + 1)
                    sp.wait_ge(ctx_lo, k - 3)
                sp.dma_start(craw[k % 4], ct[:, k, :]).then_inc(c_in_s[k % 4], 16)

        class Norm:
            def __init__(self, name, before):
                self.full = sem(f"{name}_bank_full")
                self.hi = sem(f"{name}_high_part_out")
                self.lo = sem(f"{name}_low_part_out")
                self.before = before
                self.layer = before // NT

            def pe(self, pe):
                for i in range(NT):
                    pe.wait_ge(xn_s, self.before + i + 1)
                    if i >= 4:
                        pe.wait_ge(self.lo, i - 3)
                    for c in range(ND):
                        last = nc.tensor.transpose(bank(i % 4)[:, c * P:(c + 1) * P], xn[:, i % 2, c * P:(c + 1) * P], id32[:])
                    last.then_inc(self.full, 1)

            def src(self, i):
                return bank(i % 4).rearrange("p (c t) -> p c t", c=ND)

            def act(self, act):
                root(act, self.layer)
                for i in range(NT):
                    act.wait_ge(self.full, i + 1)
                    nc.scalar.activation(xT[:, 0, :, i * P:(i + 1) * P], self.src(i), ACT.Copy).then_inc(self.hi, 1)

            def dve(self, dve):
                statistics(dve, self.layer, lambda i: None)

                def norm(i):
                    def ring_free():
                        if i >= 2:
                            dve.wait_ge(self.full, i - 1)
                    normalise(dve, i, ring_free)
                norm(0)
                norm(1)
                for i in range(NT):
                    dve.wait_ge(self.hi, i + 1)
                    nc.vector.tensor_tensor(xT[:, 1, :, i * P:(i + 1) * P], self.src(i), xT[:, 0, :, i * P:(i + 1) * P],
                                            ALU.subtract).then_inc(self.lo, 1)
                    if i + 2 < NT:
                        norm(i + 2)

        class Attention:
            def __init__(self, name, first):
                self.first = first
                self.nc_ = 3 if first else 2
                self.s_full = sem(f"{name}_scores_full")
                self.nmax_s = sem(f"{name}_negative_max")
                self.exp_s = sem(f"{name}_exp_done")
                self.hi_s = sem(f"{name}_probs_high")
                self.lo_s = sem(f"{name}_probs_low")
                self.t_full = sem(f"{name}_probs_transposed")
                self.t_act = sem(f"{name}_probs_moved_by_scalar")
                self.t_dve = sem(f"{name}_probs_moved_by_vector")
                self.pv_full = sem(f"{name}_values_full")
                self.o_f = sem(f"{name}_readout_scaled")
                self.o_hi = sem(f"{name}_readout_high")
                self.o_lo = sem(f"{name}_readout_low")
                self.ot_full = sem(f"{name}_readout_transposed")
                self.ot_out = sem(f"{name}_readout_moved")
                self.op_full = sem(f"{name}_projection_full")
                self.x_s = sem(f"{name}_x_updated")
                self.sc_s = sem(f"{name}_scores_masked")
                self.rinv_s = sem(f"{name}_sum_inverted")

            def scores(self, pe, i):
                if i >= 2:
                    pe.wait_ge(self.sc_s if not self.first else self.exp_s, i - 1)
                q = qT if self.first else xT
                b = i // TPB
                for c in range(self.nc_):
                    if c < 2:
                        mov = lambda h, d: ctxT[:, h, d, b * C + c * 512:b * C + (c + 1) * 512]
                    else:
                        mov = lambda h, d: kT[:, h, d, b * S:(b + 1) * S]
                    last = three(pe, bank(3 * (i % 2) + c), range(ND), lambda h, d: q[:, h, d, i * P:(i + 1) * P], mov)
                last.then_inc(self.s_full, 1)

            def pe(self, pe):
                self.scores(pe, 0)
                n = self.nc_
                for i in range(NT + 1):
                    if i + 1 < NT:
                        self.scores(pe, i + 1)
                    if i < NT:
                        pe.wait_ge(self.lo_s, i + 1)
                        for c in range(n):
                            if i >= 1 and c == 0 and (not self.first) and n == 2:
                                pass
                            if c == 0 and i >= 2 and self.first:
                                pe.wait_ge(self.x_s, i - 1)
                            if c == 0 and i >= 1 and not self.first:
                                pass
                            if c == 1 and i >= 1:
                                pe.wait_ge(self.o_lo if self.first else self.x_s, i)
                            if c == 2:
                                pe.wait_ge(self.t_act, 2 * i + 1)
                            for h in range(2):
                                for k in range(4):
                                    last = nc.tensor.transpose(
                                        bank16(6 + c % 2)[:, (4 * h + k) * P:(4 * h + k + 1) * P],
                                        ph[:, h, (4 * c + k) * P:(4 * c + k + 1) * P], id16[:])
                            last.then_inc(self.t_full, 1)
                    if i >= 1 and self.first:
                        j = i - 1
                        if i < NT:
                            pe.wait_ge(self.t_dve, i + 1)
                        pe.wait_ge(self.o_lo, j + 1)
                        for h in range(2):
                            for d in range(ND):
                                last = nc.tensor.transpose(bank16(7)[:, (4 * h + d) * P:(4 * h + d + 1) * P],
                                                           oh[:, h, d * P:(d + 1) * P], id16[:])
                        last.then_inc(self.ot_full, 1)
                        if i < NT:
                            pe.wait_ge(self.t_act, 2 * i + 2)
                        else:
                            pe.wait_ge(self.x_s, j)
                        pe.wait_ge(self.ot_out, j + 1)
                        three(pe, bank(6), range(ND), lambda h, d: oT[:, h, d, :],
                              lambda h, d: wT["o"][:, h, d, :]).then_inc(self.op_full, 1)
                    if i < NT:
                        b = i // TPB
                        pe.wait_ge(self.t_dve, i + 1)
                        pe.wait_ge(self.t_act, (2 if self.first else 1) * (i + 1))

                        def val(h, k):
                            return ctxN[:, h, b * CPB + k, :] if k < CPB else vN[:, h, b * TPB + k - CPB, :]
                        three(pe, bank(7 if self.first else 6), range(4 * n), lambda h, k: pT[:, h, k, :],
                              val).then_inc(self.pv_full, 1)

            def move(self, i, c):
                return pT[:, :, 4 * c:4 * c + 4, :], bank16(6 + c % 2).rearrange("p (h k q) -> p h k q", h=2, k=4)

            def act(self, act):
                n = self.nc_
                for i in range(NT):
                    act.wait_ge(self.nmax_s, i + 1)
                    if i >= 1:
                        act.wait_ge(self.lo_s, i)
                    src = bank(3 * (i % 2), n) if self.first else pf[:, 0:512 * n]
                    nc.scalar.activation(pf[:, 0:512 * n], src, ACT.Exp, bias=nmax[:, i % 2:i % 2 + 1],
                                         scale=SCALE if self.first else 1.0,
                                         accum_out=rsum[:, i % 2:i % 2 + 1]).then_inc(self.exp_s, 1)
                    act.wait_ge(self.t_full, n * i + 1)
                    if i >= 1:
                        act.wait_ge(self.pv_full, i)
                    nc.scalar.activation(*self.move(i, 0), ACT.Copy).then_inc(self.t_act, 1)
                    if self.first:
                        act.wait_ge(self.t_full, n * i + 3)
                        nc.scalar.activation(*self.move(i, 2), ACT.Copy).then_inc(self.t_act, 1)
                        act.wait_ge(self.pv_full, i + 1)
                        act.wait_ge(self.rinv_s, i + 1)
                        if i >= 1:
                            act.wait_ge(self.o_lo, i)
                            act.wait_ge(self.ot_full, i)
                        nc.scalar.activation(of, bank(7), ACT.Copy, scale=rinv[:, i % 2:i % 2 + 1]).then_inc(self.o_f, 1)
                        act.wait_ge(self.o_f, i + 1)
                        nc.scalar.activation(oh[:, 0, :], of, ACT.Copy).then_inc(self.o_hi, 1)

            def dve_out(self, dve, j):
                dve.wait_ge(self.ot_full, j + 1)
                if j >= 1:
                    dve.wait_ge(self.op_full, j)
                nc.vector.tensor_copy(oT, bank16(7).rearrange("p (h d q) -> p h d q", h=2, d=ND)).then_inc(self.ot_out, 1)
                dve.wait_ge(self.op_full, j + 1)
                nc.vector.tensor_tensor(x_sb[:, j, :], x_sb[:, j, :], bank(6), ALU.add).then_inc(self.x_s, 1)

            def dve(self, dve):
                n = self.nc_
                for i in range(NT):
                    b = i // TPB
                    dve.wait_ge(self.s_full, i + 1)
                    if self.first:
                        link(dve, nc.vector.reduce_max(rmax, bank(3 * (i % 2), n), AX_X))
                        nc.vector.tensor_scalar(nmax[:, i % 2:i % 2 + 1], rmax, -SCALE, None, ALU.mult).then_inc(self.nmax_s, 1)
                    else:
                        ins = nc.vector.scalar_tensor_tensor(pf[:, 0:512 * n], bank(3 * (i % 2), n), SCALE, mbias[:, b, :],
                                                             ALU.mult, ALU.add)
                        ins.then_inc(self.sc_s, 1)
                        dve.wait_ge(self.sc_s, i + 1)
                        link(dve, nc.vector.reduce_max(rmax, pf[:, 0:512 * n], AX_X))
                        nc.vector.tensor_scalar(nmax[:, i % 2:i % 2 + 1], rmax, -1.0, None, ALU.mult).then_inc(self.nmax_s, 1)
                    dve.wait_ge(self.exp_s, i + 1)
                    if i >= 1:
                        dve.wait_ge(self.t_full, n * i)
                    nc.vector.tensor_copy(ph[:, 0, 0:512 * n], pf[:, 0:512 * n]).then_inc(self.hi_s, 1)
                    dve.wait_ge(self.hi_s, i + 1)
                    nc.vector.tensor_tensor(ph[:, 1, 0:512 * n], pf[:, 0:512 * n], ph[:, 0, 0:512 * n],
                                            ALU.subtract).then_inc(self.lo_s, 1)
                    ri = rinv[:, i % 2:i % 2 + 1]
                    if self.first:
                        nc.vector.reciprocal(ri, rsum[:, i % 2:i % 2 + 1]).then_inc(self.rinv_s, 1)
                    else:
                        link(dve, nc.vector.reciprocal(ri, rsum[:, i % 2:i % 2 + 1]))
                        nc.vector.tensor_tensor(ri, ri, mval[:, b:b + 1], ALU.mult).then_inc(self.rinv_s, 1)
                    dve.wait_ge(self.t_full, n * i + 2)
                    if i >= 1:
                        dve.wait_ge(self.pv_full, i)
                    nc.vector.tensor_copy(*self.move(i, 1)).then_inc(self.t_dve, 1)
                    if self.first:
                        if i >= 1:
                            self.dve_out(dve, i - 1)
                        dve.wait_ge(self.o_hi, i + 1)
                        nc.vector.tensor_tensor(oh[:, 1, :], of, oh[:, 0, :], ALU.subtract).then_inc(self.o_lo, 1)
                    else:
                        dve.wait_ge(self.pv_full, i + 1)
                        dve.wait_ge(self.rinv_s, i + 1)
                        nc.vector.scalar_tensor_tensor(x_sb[:, i, :], bank(6), ri, x_sb[:, i, :], ALU.mult,
                                                       ALU.add).then_inc(self.x_s, 1)
                if self.first:
                    self.dve_out(dve, NT - 1)

        class Experts:
            def __init__(self, name, wg, wu, wd, router, K):
                self.wg, self.wu, self.wd, self.router, self.K = wg, wu, wd, router, K
                self.E, _, self.I = wg.shape
                I = self.I
                self.paired = I % P != 0
                GU = ND * 2 * I
                self.gur, self.dr, self.gu, self.d = [], [], [], []
                o = 0
                for s in range(2):
                    self.gur.append(carve(big, o, GU, F32, "p (c i) -> p c i", c=ND)); o += 2 * GU
                    self.dr.append(carve(big, o, 2 * D, F32, "p (c n) -> p c n", c=2)); o += 4 * D
                    self.gu.append(carve(big, o, 2 * GU, F16, "p (h c i) -> p h c i", h=2, c=ND)); o += 2 * GU
                    self.d.append(carve(big, o, 4 * D, F16, "p (h c n) -> p h c n", h=2, c=2)); o += 4 * D
                self.NTR = 3 if self.paired else 4
                o = 0
                self.sil = [carve(mid, o + s * 512, 256, F32)[:, 0:I] for s in range(2)]; o += 1024
                self.h = [carve(mid, o + s * 512, 256, F32)[:, 0:I] for s in range(2)]; o += 1024
                self.hs = [carve(mid, o + s * 512, 512, F16) for s in range(2)]; o += 1024
                self.hT = [carve(mid, o + s * 512, 512, F16, "p (c t) -> p c t", t=P) for s in range(2)]; o += 1024
                E = self.E
                def rt(k):
                    return carve(mid, 4096 + 512 * k, NT * E, F32, "p (t e) -> p t e", t=NT)
                self.lg, self.pr, self.m, self.w, self.w2 = rt(0), rt(1), rt(2), rt(3), rt(4)
                self.top = carve(mid, 4096 + 5 * 512, NT * 8, F32, "p (t e) -> p t e", t=NT)
                self.idx = carve(mid, 4096 + 5 * 512 + 128, NT * 8, U32, "p (t e) -> p t e", t=NT)
                self.idf = carve(mid, 4096 + 5 * 512 + 256, NT * 8, F32, "p (t e) -> p t e", t=NT)
                self.io = carve(mid, 4096 + 5 * 512 + 384, E, F32)
                self.s8 = carve(mid, 4096 + 5 * 512 + 448, NT, F32)
                self.s8b = carve(mid, 4096 + 5 * 512 + 464, NT, F32)
                def two(what):
                    return [sem(f"{name}_{what}_{i}") for i in range(2)]

                self.gate_in, self.up_in, self.down_in = two("gate_loaded"), two("up_loaded"), two("down_loaded")
                self.rest_in, self.rest2_in = two("down_rest_loaded"), two("down_rest_loaded_again")
                self.w_hi = sem(f"{name}_weight_high_parts")
                self.w_lo = sem(f"{name}_weight_low_parts")
                self.zeroed = sem(f"{name}_low_rest_padded")
                self.iota_s = sem(f"{name}_expert_numbers")
                self.lg_full = sem(f"{name}_logits_full")
                self.lg_out = sem(f"{name}_logits_shifted")
                self.routed = sem(f"{name}_logits_exponentiated")
                self.gu_full = sem(f"{name}_gate_up_full")
                self.sil_s = sem(f"{name}_silu_done")
                self.h_s = sem(f"{name}_h_done")
                self.hhi_s = sem(f"{name}_h_high")
                self.hlo_s = sem(f"{name}_h_low")
                self.t_full = sem(f"{name}_h_transposed")
                self.ht_s = sem(f"{name}_h_transposed_moved")
                self.d_full = sem(f"{name}_down_full")
                self.x_s = sem(f"{name}_x_updated")
                self.NL = self.E // 2

            def load(self, sp, e, s):
                sp.dma_start(self.gur[s][:, :, 0:self.I], self.wg[e, :, :].rearrange("(c p) i -> p c i", p=P)).then_inc(self.gate_in[s], 16)
                sp.dma_start(self.gur[s][:, :, self.I:], self.wu[e, :, :].rearrange("(c p) i -> p c i", p=P)).then_inc(self.up_in[s], 16)
                if self.paired:
                    R = self.I - P
                    sp.dma_start(self.dr[s][:, 0, :], self.wd[e, 0:P, :]).then_inc(self.down_in[s], 16)
                    sp.dma_start(self.dr[s][0:R, 1, :], self.wd[e, P:self.I, :]).then_inc(self.rest_in[s], 16)
                    sp.dma_start(self.dr[s][P - R:P, 1, :], self.wd[e, P:self.I, :]).then_inc(self.rest2_in[s], 16)
                else:
                    sp.dma_start(self.dr[s], self.wd[e, :, :].rearrange("(c p) n -> p c n", p=P)).then_inc(self.down_in[s], 16)

            def sp(self, sp):
                self.load(sp, 0, 0)
                self.load(sp, 1, 1)
                with sp.Fori(1, self.NL) as it:
                    for s in range(2):
                        sp.wait_ge(self.w_lo, 2 * it + s - 1)
                        self.load(sp, 2 * it + s, s)

            def split_hi(self, act, it, s, guard):
                for q in (self.gate_in, self.up_in, self.down_in) + ((self.rest_in, self.rest2_in) if self.paired else ()):
                    act.wait_ge(q[s], 16 * it + 16)
                if guard:
                    act.wait_ge(self.d_full, 8 * (2 * it + s) - 8)
                nc.scalar.activation(self.gu[s][:, 0, :, :], self.gur[s], ACT.Copy).then_inc(self.w_hi, 1)
                nc.scalar.activation(self.d[s][:, 0, :, :], self.dr[s], ACT.Copy).then_inc(self.w_hi, 1)

            def split_lo(self, pool, it, s):
                pool.wait_ge(self.w_hi, 2 * (2 * it + s) + 2)
                nc.gpsimd.tensor_tensor(self.gu[s][:, 1, :, :], self.gur[s], self.gu[s][:, 0, :, :], ALU.subtract)
                if self.paired:
                    R = self.I - P
                    nc.gpsimd.tensor_tensor(self.d[s][:, 1, 0, :], self.dr[s][:, 0, :], self.d[s][:, 0, 0, :], ALU.subtract)
                    last = nc.gpsimd.tensor_tensor(self.d[s][0:R, 1, 1, :], self.dr[s][0:R, 1, :], self.d[s][0:R, 0, 1, :], ALU.subtract)
                else:
                    last = nc.gpsimd.tensor_tensor(self.d[s][:, 1, :, :], self.dr[s], self.d[s][:, 0, :, :], ALU.subtract)
                last.then_inc(self.w_lo, 1)

            def pool(self, pool, ready):
                nc.gpsimd.iota(self.io, pattern=[[1, self.E]], base=0, channel_multiplier=0,
                               allow_small_or_imprecise_dtypes=True).then_inc(self.iota_s, 1)
                if self.paired:
                    pool.wait_ge(self.iota_s, 1)
                    for s in range(2):
                        nc.gpsimd.memset(self.d[s][self.I - P:P, 1, 1, :], 0.0).then_inc(self.zeroed, 1)
                    pool.wait_ge(self.zeroed, 2)
                self.split_lo(pool, 0, 0)
                self.split_lo(pool, 0, 1)
                with pool.Fori(1, self.NL) as it:
                    for s in range(2):
                        self.split_lo(pool, it, s)

            def gate_up(self, pe, n, k):
                s, tt = (k // 8) % 2, k % 8
                three(pe, bank(k % 2)[:, 0:2 * self.I], range(ND), lambda h, d: xT[:, h, d, tt * P:(tt + 1) * P],
                      lambda h, d: self.gu[s][:, h, d, :]).then_inc(self.gu_full, 1)

            def turn(self, pe, n, k):
                for c in range(self.NTR):
                    last = nc.tensor.transpose(bank16(2 + k % 2)[:, c * P:(c + 1) * P], self.hs[k % 2][:, c * P:(c + 1) * P], id16[:])
                last.then_inc(self.t_full, 1)

            def down(self, pe, n, k):
                s = k // 8
                w, hT = self.d[s], self.hT[k % 2]
                if self.paired:
                    seq = [(0, 0, 0), (0, 1, 0), (1, 0, 0), (2, 0, 1), (2, 1, 1)]
                else:
                    seq = [(0, 0, 0), (0, 1, 0), (1, 0, 1), (1, 1, 1), (2, 0, 0), (3, 0, 1)]
                for q, (t, h, c) in enumerate(seq):
                    last = nc.tensor.matmul(bank(4 + k % 2), hT[:, t, :], w[:, h, c, :], start=(q == 0), stop=(q == len(seq) - 1))
                last.then_inc(self.d_full, 1)

            def pe_route(self, pe):
                E = self.E
                for t in range(NT):
                    last = three(pe, bank(7)[:, t * E:(t + 1) * E], range(ND), lambda h, d: xT[:, h, d, t * P:(t + 1) * P],
                                 lambda h, d: self.router[:, h, d, :])
                last.then_inc(self.lg_full, 1)

            def pe(self, pe):
                self.pe_route(pe)
                pe.wait_ge(self.w_lo, 1)
                if self.paired:
                    pe.wait_ge(self.zeroed, 2)
                self.gate_up(pe, 0, 0)
                self.gate_up(pe, 1, 1)
                pe.wait_ge(self.hlo_s, 1)
                self.turn(pe, 0, 0)

                def step(it, first, last):
                    for k in range(16):
                        n = 16 * it + k
                        if k < 14 or not last:
                            if k == 6 or k == 14:
                                pe.wait_ge(self.w_lo, 2 * it + k // 8 + 2)
                            pe.wait_ge(self.h_s, n + 1)
                            self.gate_up(pe, n + 2, k + 2)
                        if k < 15 or not last:
                            pe.wait_ge(self.hlo_s, n + 2)
                            if not (first and k == 0):
                                pe.wait_ge(self.ht_s, n)
                            self.turn(pe, n + 1, k + 1)
                        pe.wait_ge(self.ht_s, n + 1)
                        if not (first and k < 2):
                            pe.wait_ge(self.x_s, n - 1)
                        self.down(pe, n, k)
                step(0, True, False)
                if self.NL > 2:
                    with pe.Fori(1, self.NL - 1) as it:
                        step(it, False, False)
                step(self.NL - 1, False, True)

            def act(self, act):
                self.split_hi(act, 0, 0, False)

                def moveT(n, k):
                    act.wait_ge(self.t_full, n + 1)
                    nc.scalar.activation(self.hT[k % 2][:, 0:self.NTR, :],
                                         bank16(2 + k % 2)[:, 0:self.NTR * P].rearrange("p (c t) -> p c t", t=P),
                                         ACT.Copy).then_inc(self.ht_s, 1)

                def step(it, first, last):
                    for k in range(16):
                        n = 16 * it + k
                        act.wait_ge(self.gu_full, n + 1)
                        if not (first and k < 2):
                            act.wait_ge(self.h_s, n - 1)
                        nc.scalar.activation(self.sil[k % 2], bank(k % 2)[:, 0:self.I], ACT.Silu).then_inc(self.sil_s, 1)
                        if not (first and k == 0):
                            if not (first and k <= 2):
                                act.wait_ge(self.d_full, n - 2)
                            moveT(n - 1, k + 1)
                        if k == 2:
                            self.split_hi(act, it, 1, not first)
                        if k == 10 and not last:
                            self.split_hi(act, it + 1, 0, True)
                step(0, True, False)
                if self.NL > 2:
                    with act.Fori(1, self.NL - 1) as it:
                        step(it, False, False)
                step(self.NL - 1, False, True)
                act.wait_ge(self.d_full, 8 * self.E - 2)
                moveT(8 * self.E - 1, 1)

            def dve_route(self, dve):
                E, K = self.E, self.K
                dve.wait_ge(self.lg_full, 1)
                link(dve, nc.vector.tensor_copy(self.lg, bank(7)[:, 0:NT * E].rearrange("p (t e) -> p t e", t=NT)))
                for t in range(NT):
                    last = nc.vector.max(self.top[:, t, :], self.lg[:, t, :])
                link(dve, last)
                if K == 8:
                    for t in range(NT):
                        last = nc.vector.match_replace(self.m[:, t, :], self.top[:, t, :], self.lg[:, t, :], -3e38)
                    link(dve, last)
                    link(dve, nc.vector.tensor_tensor(self.m, self.m, self.lg, ALU.not_equal))
                else:
                    for t in range(NT):
                        last = nc.vector.max_index(self.idx[:, t, :], self.top[:, t, :], self.lg[:, t, :])
                    link(dve, last)
                    link(dve, nc.vector.tensor_copy(self.idf, self.idx))
                    dve.wait_ge(self.iota_s, 1)
                    for t in range(NT):
                        nc.vector.tensor_scalar(self.m[:, t, :], self.io, self.idf[:, t, 0:1], None, ALU.is_equal)
                        last = nc.vector.tensor_scalar(self.w[:, t, :], self.io, self.idf[:, t, 1:2], None, ALU.is_equal)
                    link(dve, last)
                    link(dve, nc.vector.tensor_tensor(self.m, self.m, self.w, ALU.add))
                link(dve, nc.vector.tensor_tensor(self.pr, self.lg, self.top[:, :, 0:1].to_broadcast([P, NT, E]), ALU.subtract))
                self.lg_out_n = 1
                nc.vector.tensor_copy(self.lg, self.pr).then_inc(self.lg_out, 1)
                dve.wait_ge(self.routed, 1)
                if K == 8:
                    link(dve, nc.vector.tensor_reduce(self.s8, self.lg, AX_X, ALU.add))
                    link(dve, nc.vector.reciprocal(self.s8, self.s8))
                    link(dve, nc.vector.tensor_tensor(self.lg, self.lg, self.s8.unsqueeze(2).to_broadcast([P, NT, E]), ALU.mult))
                link(dve, nc.vector.tensor_tensor(self.w, self.lg, self.m, ALU.mult))
                link(dve, nc.vector.tensor_reduce(self.s8, self.w, AX_X, ALU.add))
                if K == 8:
                    link(dve, nc.vector.tensor_scalar(self.s8, self.s8, 1e-9, None, ALU.max))
                link(dve, nc.vector.reciprocal(self.s8, self.s8))
                link(dve, nc.vector.tensor_tensor(self.w, self.w, self.s8.unsqueeze(2).to_broadcast([P, NT, E]), ALU.mult))

            def act_route(self, act):
                act.wait_ge(self.lg_out, 1)
                nc.scalar.activation(self.lg, self.pr, ACT.Exp).then_inc(self.routed, 1)

            def dve(self, dve):
                self.dve_route(dve)
                I = self.I

                def add(n, k, e):
                    tt = k % 8
                    dve.wait_ge(self.d_full, n + 1)
                    nc.vector.scalar_tensor_tensor(x_sb[:, tt, :], bank(4 + k % 2), self.w[:, tt, bass.ds(e, 1)], x_sb[:, tt, :],
                                                   ALU.mult, ALU.add).then_inc(self.x_s, 1)

                def step(it, first, last):
                    for k in range(16):
                        n = 16 * it + k
                        dve.wait_ge(self.sil_s, n + 1)
                        nc.vector.tensor_tensor(self.h[k % 2], self.sil[k % 2], bank(k % 2)[:, I:2 * I], ALU.mult).then_inc(self.h_s, 1)
                        dve.wait_ge(self.h_s, n + 1)
                        if not (first and k < 2):
                            dve.wait_ge(self.t_full, n - 1)
                        hs, h = self.hs[k % 2], self.h[k % 2]
                        if self.paired:
                            hi = hs[:, 0:4 * P].rearrange("p (a b) -> p a b", a=2)
                            nc.vector.tensor_copy(hs[:, 0:P], h[:, 0:P])
                            nc.vector.tensor_copy(hs[:, 2 * P:2 * P + I - P], h[:, P:I]).then_inc(self.hhi_s, 1)
                            dve.wait_ge(self.hhi_s, n + 1)
                            nc.vector.tensor_tensor(hs[:, P:2 * P], h[:, 0:P], hs[:, 0:P], ALU.subtract)
                            nc.vector.tensor_tensor(hs[:, 2 * P + I - P:3 * P], h[:, P:I], hs[:, 2 * P:2 * P + I - P],
                                                    ALU.subtract).then_inc(self.hlo_s, 1)
                        else:
                            nc.vector.tensor_copy(hs[:, 0:I], h).then_inc(self.hhi_s, 1)
                            dve.wait_ge(self.hhi_s, n + 1)
                            nc.vector.tensor_tensor(hs[:, I:2 * I], h, hs[:, 0:I], ALU.subtract).then_inc(self.hlo_s, 1)
                        if not (first and k < 2):
                            add(n - 2, k - 2 if k >= 2 else k + 14, 2 * it + (k - 2) // 8)
                step(0, True, False)
                if self.NL > 2:
                    with dve.Fori(1, self.NL - 1) as it:
                        step(it, False, False)
                step(self.NL - 1, False, True)
                add(8 * self.E - 2, 14, self.E - 1)
                add(8 * self.E - 1, 15, self.E - 1)

        attn0 = Attention("attn0", True)
        attn1 = Attention("attn1", False)
        exp0 = Experts("moe0", wi0, wi1, wo0, g0[:], 2)
        exp1 = Experts("moe1", wg1, wu1, wd1, g1T[:], 8)
        norm1, norm2, norm3 = Norm("norm1", NT), Norm("norm2", 2 * NT), Norm("norm3", 3 * NT)
        out_s = sem("output_stored")
        mask_s = sem("mask_bias_ready")

        block = ctx.enter_context(nc.Block())

        @block.sync
        def _(sp):
            sp_prep(sp)
            sp.wait_ge(attn0.x_s, NT)
            exp0.sp(sp)
            sp.wait_ge(exp0.x_s, NT * E0)
            for b in range(B):
                sp.dma_start(mraw[:, b, :], mask_in[b, :].partition_broadcast(P)).then_inc(m_in_s, 16)
            exp1.sp(sp)
            sp.wait_ge(exp1.x_s, NT * E1)
            ot = out.rearrange("b (t p) d -> p (b t) d", p=P)
            for i in range(NT):
                sp.dma_start(ot[:, i, :], x_sb[:, i, :]).then_inc(out_s, 16)
            sp.wait_ge(out_s, 16 * NT)

        @block.gpsimd
        def _(pool):
            pool_prep(pool)
            pool.wait_ge(norm1.lo, NT)
            exp0.pool(pool, None)
            pool.wait_ge(norm3.lo, NT)
            exp1.pool(pool, None)

        @block.scalar
        def _(act):
            act_prep(act)
            attn0.act(act)
            norm1.act(act)
            exp0.act_route(act)
            exp0.act(act)
            norm2.act(act)
            attn1.act(act)
            norm3.act(act)
            exp1.act_route(act)
            exp1.act(act)

        @block.tensor
        def _(pe):
            pe_prep(pe)
            pe.wait_ge(prep_lo, NPREP)
            pe.wait_ge(ctx_lo, NCT)
            attn0.pe(pe)
            norm1.pe(pe)
            pe.wait_ge(norm1.lo, NT)
            pe.wait_ge(g0_s, 1)
            exp0.pe(pe)
            norm2.pe(pe)
            pe.wait_ge(norm2.lo, NT)
            attn1.pe(pe)
            norm3.pe(pe)
            pe.wait_ge(norm3.lo, NT)
            exp1.pe(pe)

        @block.vector
        def _(dve):
            dve_prep(dve)
            attn0.dve(dve)
            dve.wait_ge(attn0.x_s, NT)
            norm1.dve(dve)
            exp0.dve(dve)
            dve.wait_ge(exp0.x_s, NT * E0)
            norm2.dve(dve)
            dve.wait_ge(m_in_s, 16 * B)
            link(dve, nc.vector.tensor_scalar(mbias, mraw, 1.0, NEG, ALU.subtract, ALU.mult))
            link(dve, nc.vector.tensor_reduce(mval, mbias, AX_X, ALU.max))
            link(dve, nc.vector.tensor_scalar(mval, mval, -0.5, None, ALU.is_ge))
            attn1.dve(dve)
            dve.wait_ge(attn1.x_s, NT)
            norm3.dve(dve)
            exp1.dve(dve)


_INS = ['x', 'ctx_2048', 'mask_BxS2_bk0', 'L0_xattn_wq', 'L0_xattn_wk', 'L0_xattn_wv', 'L0_xattn_wo',
        'L0_ffn_w_gate', 'L0_ffn_wi_0', 'L0_ffn_wi_1', 'L0_ffn_wo', 'L1_ffn_gate_w', 'L1_ffn_w_gate',
        'L1_ffn_w_up', 'L1_ffn_w_down']
_OUTS = [((2, 512, 512), 'float32')]


def kernel(**inputs):
    import numpy as _np
    import concourse.bacc as _bacc
    from concourse import mybir as _mybir
    from concourse.bass_utils import run_bass_kernel_spmd as _run

    nc = _bacc.Bacc("TRN2", target_bir_lowering=False, num_devices=1)
    arrays, args = {}, []
    for name in _INS:
        a = _np.ascontiguousarray(inputs[name])
        arrays[f"in_{name}_dram"] = a
        args.append(nc.dram_tensor(f"in_{name}_dram", a.shape, _mybir.dt.from_np(a.dtype), kind="ExternalInput").ap())
    for i, (shape, dtype) in enumerate(_OUTS):
        dt = _mybir.dt.from_np(_np.dtype(dtype))
        args.append(nc.dram_tensor(f"out_{i}_dram", shape, dt, kind="ExternalOutput").ap())
    program(nc, *args)
    r = _run(nc, [arrays], core_ids=[0])
    got = tuple(r.results[0][f"out_{i}_dram"] for i in range(len(_OUTS)))
    return got[0]
```
